# Optimizing a Trainium2 kernel written in Bass

```python
import numpy as np
import jax
import jax.numpy as jnp

def _softmax(x, axis=-1):
    return jax.nn.softmax(x, axis=axis)

def _gelu(x):
    return jax.nn.gelu(x, approximate=True)

def _silu(x):
    return jax.nn.silu(x)

def _sigmoid(x):
    return jax.nn.sigmoid(x)

def _layernorm(x, axis=-1, eps=1e-05):
    m = jnp.mean(x, axis=axis, keepdims=True)
    v = jnp.var(x, axis=axis, keepdims=True)
    return (x - m) / jnp.sqrt(v + eps)

def _scatter_add(tgt, idx, src, axis=0):
    return tgt.at[idx].add(src)

def _segment_sum(src, seg, n):
    return jax.ops.segment_sum(src, seg, n)
kernel_name = 'mk_vit_tower_d1_tok_img768_r4_17e925'

def setup_inputs(seed: int=0):
    np.random.seed(seed)
    _w = jnp.asarray

    def _rec_inputs():
        import jax
        import jax.numpy as jnp
        _rk = jax.random.key(seed)
        x = 7.57192e-06 + 1.00007 * jax.random.normal(jax.random.fold_in(_rk, 1), (64, 224, 224, 3), jnp.float32)
        return x
    x = _rec_inputs()

    def _L0_tok_setup():
        import jax, jax.numpy as jnp
        import numpy as np
        IMG = 224
        P = 16
        HP = P // 2
        D = 192
        C_IN = 3
        B = 64

        def _crop_shift_pad(images, oh, ow):
            th = IMG - HP
            tw = IMG - HP
            out = jnp.zeros_like(images)
            return out.at[:, oh:oh + th, ow:ow + tw, :].set(images[:, oh:oh + th, ow:ow + tw, :])
        key = jax.random.key(seed)
        k1, k2 = jax.random.split(key, 2)
        images = jax.random.normal(k1, (B, IMG, IMG, C_IN), dtype=jnp.float32)
        pvs = P * P * C_IN * 5
        W = jax.random.normal(k2, (pvs, D), dtype=jnp.float32) * 0.02
        b = jnp.zeros((D,), dtype=jnp.float32)
        return {'images': images, 'W': W, 'b': b}
    _L0_tok_all = _L0_tok_setup()
    _L0_tok_in = {k: v for k, v in _L0_tok_all.items() if k in ('W', 'b')}
    del _L0_tok_all

    def _L0_attn_setup():
        import jax, jax.numpy as jnp
        import numpy as np
        N_HEAD = 12
        key = jax.random.key(seed)
        ks = jax.random.split(key, 6)
        B, T, C = (8, 256, 192)
        x = jax.random.normal(ks[0], (B, T, C), dtype=jnp.float32)
        w_attn = jax.random.normal(ks[1], (C, 3 * C), dtype=jnp.float32) * 0.02
        b_attn = jnp.zeros((3 * C,), dtype=jnp.float32)
        w_proj = jax.random.normal(ks[2], (C, C), dtype=jnp.float32) * 0.02
        b_proj = jnp.zeros((C,), dtype=jnp.float32)
        rel_emb = jax.random.normal(ks[3], (2 * 256 - 1, C // N_HEAD), dtype=jnp.float32) * 0.02
        return {'x': x, 'w_attn': w_attn, 'b_attn': b_attn, 'w_proj': w_proj, 'b_proj': b_proj, 'rel_emb': rel_emb}
    _L0_attn_all = _L0_attn_setup()
    _L0_attn_in = {k: v for k, v in _L0_attn_all.items() if k in ('w_attn', 'b_attn', 'w_proj', 'b_proj', 'rel_emb')}
    del _L0_attn_all

    def _L0_ffn_setup():
        import jax, jax.numpy as jnp
        import numpy as np
        import math
        B, T, C = (8, 512, 192)
        E = 3
        HD = C // E
        TOPK = 2
        NGLOB = 4

        def _masked_softmax(att, mask):
            att = jnp.where(mask, -jnp.inf, att)
            return jax.nn.softmax(att, axis=-1)
        key = jax.random.key(seed)
        ks = jax.random.split(key, 16)
        s = 0.02
        return {'x': jax.random.normal(ks[0], (B, T, C), jnp.float32), 'Wqk': jax.random.normal(ks[1], (C, 2 * C), jnp.float32) * s, 'bqk': jnp.zeros((2 * C,), jnp.float32), 'Wv': jax.random.normal(ks[2], (E, C, HD), jnp.float32) * s, 'bv': jnp.zeros((E, HD), jnp.float32), 'conv_w': jax.random.normal(ks[3], (HD, 1, 3), jnp.float32) * s, 'conv_b': jnp.zeros((HD,), jnp.float32), 'glob': jax.random.normal(ks[4], (NGLOB, HD), jnp.float32) * 0.02, 'pos_bias': jnp.zeros((64, 64), jnp.float32), 'Wg1': jax.random.normal(ks[5], (C, 32), jnp.float32) * s, 'bg1': jnp.zeros((32,), jnp.float32), 'Wg2': jax.random.normal(ks[6], (32, E), jnp.float32) * s, 'bg2': jnp.zeros((E,), jnp.float32), 'Wp': jax.random.normal(ks[7], (C, C), jnp.float32) * s, 'bp': jnp.zeros((C,), jnp.float32)}
    _L0_ffn_all = _L0_ffn_setup()
    _L0_ffn_in = {k: v for k, v in _L0_ffn_all.items() if k in ('Wqk', 'bqk', 'Wv', 'bv', 'conv_w', 'conv_b', 'glob', 'pos_bias', 'Wg1', 'bg1', 'Wg2', 'bg2', 'Wp', 'bp')}
    del _L0_ffn_all
    return {'x': x, 'L0_tok_W': _L0_tok_in['W'], 'L0_tok_b': _L0_tok_in['b'], 'L0_attn_w_attn': _L0_attn_in['w_attn'], 'L0_attn_b_attn': _L0_attn_in['b_attn'], 'L0_attn_w_proj': _L0_attn_in['w_proj'], 'L0_attn_b_proj': _L0_attn_in['b_proj'], 'L0_attn_rel_emb': _L0_attn_in['rel_emb'], 'L0_ffn_Wqk': _L0_ffn_in['Wqk'], 'L0_ffn_bqk': _L0_ffn_in['bqk'], 'L0_ffn_Wv': _L0_ffn_in['Wv'], 'L0_ffn_bv': _L0_ffn_in['bv'], 'L0_ffn_conv_w': _L0_ffn_in['conv_w'], 'L0_ffn_conv_b': _L0_ffn_in['conv_b'], 'L0_ffn_glob': _L0_ffn_in['glob'], 'L0_ffn_pos_bias': _L0_ffn_in['pos_bias'], 'L0_ffn_Wg1': _L0_ffn_in['Wg1'], 'L0_ffn_bg1': _L0_ffn_in['bg1'], 'L0_ffn_Wg2': _L0_ffn_in['Wg2'], 'L0_ffn_bg2': _L0_ffn_in['bg2'], 'L0_ffn_Wp': _L0_ffn_in['Wp'], 'L0_ffn_bp': _L0_ffn_in['bp']}

def reference(x, L0_tok_W, L0_tok_b, L0_attn_w_attn, L0_attn_b_attn, L0_attn_w_proj, L0_attn_b_proj, L0_attn_rel_emb, L0_ffn_Wqk, L0_ffn_bqk, L0_ffn_Wv, L0_ffn_bv, L0_ffn_conv_w, L0_ffn_conv_b, L0_ffn_glob, L0_ffn_pos_bias, L0_ffn_Wg1, L0_ffn_bg1, L0_ffn_Wg2, L0_ffn_bg2, L0_ffn_Wp, L0_ffn_bp):
    import jax
    import jax.numpy as jnp

    def _L0_tok_ref(images, W, b):
        import jax, jax.numpy as jnp
        import numpy as np
        IMG = 224
        P = 16
        HP = P // 2
        D = 192
        C_IN = 3
        B = 64

        def _crop_shift_pad(images, oh, ow):
            th = IMG - HP
            tw = IMG - HP
            out = jnp.zeros_like(images)
            return out.at[:, oh:oh + th, ow:ow + tw, :].set(images[:, oh:oh + th, ow:ow + tw, :])
        offsets = [(0, 0), (HP, 0), (0, HP), (HP, HP)]
        concat = jnp.concatenate([images] + [_crop_shift_pad(images, oh, ow) for oh, ow in offsets], axis=-1)
        Bn, _, _, C = concat.shape
        g = IMG // P
        x = concat.reshape(Bn, g, P, g, P, C)
        x = x.transpose(0, 1, 3, 2, 4, 5).reshape(Bn, g * g, P * P * C)
        return x @ W + b

    def _L0_attn_ref(x, w_attn, b_attn, w_proj, b_proj, rel_emb):
        import jax, jax.numpy as jnp
        import numpy as np
        N_HEAD = 12
        b, t, c = x.shape
        h = N_HEAD
        d = c // h
        scale = d ** (-0.5)
        qkv = x @ w_attn + b_attn
        q, k, v = jnp.split(qkv, 3, axis=-1)
        split_heads = lambda z: z.reshape(b, t, h, d).transpose(0, 2, 1, 3)
        q, k, v = map(split_heads, (q, k, v))
        q = q * scale
        scores = jnp.einsum('bhid,bhjd->bhij', q, k)
        rel = rel_emb[:t]
        rel = jnp.concatenate([jnp.zeros_like(rel[:1]), rel], axis=0)[:-1]
        scores = scores + jnp.einsum('bhid,jd->bhij', q, rel)
        causal = jnp.tril(jnp.ones((t, t), dtype=bool))
        scores = jnp.where(causal, scores, -jnp.inf)
        probs = jax.nn.softmax(scores, axis=-1)
        y = jnp.einsum('bhij,bhjd->bhid', probs, v)
        y = y.transpose(0, 2, 1, 3).reshape(b, t, c)
        return y @ w_proj + b_proj

    def _L0_ffn_ref(x, Wqk, bqk, Wv, bv, conv_w, conv_b, glob, pos_bias, Wg1, bg1, Wg2, bg2, Wp, bp):
        import jax, jax.numpy as jnp
        import numpy as np
        import math
        B, T, C = (8, 512, 192)
        E = 3
        HD = C // E
        TOPK = 2
        NGLOB = 4

        def _masked_softmax(att, mask):
            att = jnp.where(mask, -jnp.inf, att)
            return jax.nn.softmax(att, axis=-1)
        Bx, Tx, Cx = x.shape
        scale = 1.0 / math.sqrt(HD)
        gate = jax.nn.softmax(jax.nn.relu(x @ Wg1 + bg1) @ Wg2 + bg2, axis=-1)
        top_w, top_i = jax.lax.top_k(gate, TOPK)
        top_w = jax.nn.softmax(top_w, axis=-1)
        qk = x @ Wqk + bqk
        q, k = (qk[..., :Cx], qk[..., Cx:])
        q = q.reshape(Bx, Tx, E, HD)
        k = k.reshape(Bx, Tx, E, HD)
        rows = jnp.arange(Tx)[:, None]
        ys = []
        for e in range(E):
            qe = q[:, :, e]
            ke = k[:, :, e]
            ve = x @ Wv[e] + bv[e]
            if e == 0:
                qc = jnp.transpose(qe, (0, 2, 1))
                qc = jax.lax.conv_general_dilated(qc, conv_w, window_strides=(1,), padding=((1, 1),), feature_group_count=HD, dimension_numbers=('NCH', 'OIH', 'NCH'))
                qe = jnp.transpose(qc + conv_b[None, :, None], (0, 2, 1))
            elif e == 1:
                gb = jnp.broadcast_to(glob[None], (Bx, NGLOB, HD))
                ke = jnp.concatenate([ke, gb], axis=1)
                ve = jnp.concatenate([ve, gb], axis=1)
            att = jnp.einsum('btd,bsd->bts', qe, ke) * scale
            if e == 2 and Tx <= 64:
                att = att + pos_bias[:Tx, :Tx][None]
            S = att.shape[-1]
            mask = jnp.arange(S)[None, :] > rows
            att = _masked_softmax(att, mask[None])
            ys.append(jnp.einsum('bts,bsd->btd', att, ve))
        ys = jnp.stack(ys, axis=2)
        w_e = jnp.sum(jax.nn.one_hot(top_i, E, dtype=x.dtype) * top_w[..., None], axis=-2)
        combined = (ys * w_e[..., None]).reshape(Bx, Tx, Cx)
        return combined @ Wp + bp
    h = _L0_tok_ref(x, L0_tok_W, L0_tok_b)
    h = h + _L0_attn_ref(_layernorm(h, axis=-1), L0_attn_w_attn, L0_attn_b_attn, L0_attn_w_proj, L0_attn_b_proj, L0_attn_rel_emb)
    h = h + _L0_ffn_ref(_layernorm(h, axis=-1), L0_ffn_Wqk, L0_ffn_bqk, L0_ffn_Wv, L0_ffn_bv, L0_ffn_conv_w, L0_ffn_conv_b, L0_ffn_glob, L0_ffn_pos_bias, L0_ffn_Wg1, L0_ffn_bg1, L0_ffn_Wg2, L0_ffn_bg2, L0_ffn_Wp, L0_ffn_bp)
    return h

_drawn_inputs = setup_inputs


def setup_inputs(seed=0):
    import zlib

    import numpy as np

    out = dict(_drawn_inputs(seed))
    spreads = {'L0_tok_b': (0.0, 0.1),
     'L0_attn_b_attn': (0.0, 0.328),
     'L0_attn_b_proj': (0.0, 0.1),
     'L0_ffn_bqk': (0.0, 0.8),
     'L0_ffn_bv': (0.0, 0.8),
     'L0_ffn_conv_b': (0.0, 0.8),
     'L0_ffn_pos_bias': (0.0, 0.1),
     'L0_ffn_bg1': (0.0, 0.8),
     'L0_ffn_bg2': (0.0, 0.793),
     'L0_ffn_bp': (0.0, 0.1)}
    factors = {'L0_attn_w_attn': 4.622,
     'L0_attn_rel_emb': 8.0,
     'L0_ffn_Wqk': 8.0,
     'L0_ffn_Wv': 8.0,
     'L0_ffn_conv_w': 8.0,
     'L0_ffn_Wg1': 8.0,
     'L0_ffn_Wg2': 8.0,
     'L0_ffn_Wp': 5.313}
    for name, (base, spread) in spreads.items():
        noise = np.random.default_rng([zlib.crc32(name.encode()), seed]).standard_normal(out[name].shape)
        drawn = base * np.exp(spread * noise) if base else spread * noise
        out[name] = jnp.asarray(drawn.astype(out[name].dtype))
    for name, factor in factors.items():
        out[name] = (out[name] * factor).astype(out[name].dtype)
    return out
```

```python
from contextlib import ExitStack

import concourse.bass as bass
from concourse import mybir

ALU = mybir.AluOpType
ACT = mybir.ActivationFunctionType
AX_X = mybir.AxisListType.X
F32 = mybir.dt.float32
BF16 = mybir.dt.bfloat16

IMAGES = 64
GRID = 14
T = GRID * GRID
TB = T // 2
D = 192
DH = D // 2
HEADS, HD = 12, 16
H6 = HEADS // 2
E, ED = 3, 64
GATE = 32
EPS = 1e-5
STACK = 6 * HD
PARTS = 3
COPIES = 5

GROUP = 8
GROUPS = IMAGES // GROUP
INNER = GRID - 2
TILE = GROUP * INNER
SUBS = 4
PER_SUB = 4
CHUNKS = 6
CH = 128

TILE_CLASS = [("M", "M")] * INNER + [("F", "M"), ("L", "M"), ("M", "F"), ("M", "L")]
CORNERS = [("F", "F"), ("F", "L"), ("L", "F"), ("L", "L")]
CORNER_AT = {"F": 0, "L": GRID - 1}

VARIANTS = sorted(((rh, rv, c3, cv) for rh in range(2) for rv in range(2) for c3 in range(3)
                   for cv in range(3 if c3 == 1 else 2)), key=lambda v: (v[1] + v[3] > 0, v))
PLAIN = sum(v[1] + v[3] == 0 for v in VARIANTS)


def variant(rc, cc, chunk):
    rh, c3 = divmod(chunk, 3)
    rv = int((rh, rc) in ((0, "F"), (1, "L")))
    cv = [int(cc == "F"), "MFL".index(cc), int(cc == "L")][c3]
    return VARIANTS.index((rh, rv, c3, cv))


W97 = dict(wq=2 * D, wk=2 * D, wv=2 * D, wproj=2 * D, fqk=2 * 3 * 128, fvg=2 * (D + GATE), wp=2 * D, rel=2 * T)
W128 = dict(ident=128, maskn=4 * TB, maskt=3 * TB, sel=E * TB, tokb=2 * D, conv=4, wg2=E * GATE, bg2=2 * E,
            keep=len(VARIANTS) * 4)


def columns(widths):
    at, out = 0, {}
    for name, w in widths.items():
        out[name] = slice(at, at + w)
        at += w
    return out, at


C97, N97 = columns(W97)
C128, N128 = columns(W128)

NEXT, A, B, C, DE, F = -1, 0, 1, 2, 3, 4
LAST = F
QUAD = 4
PRE = 2
TURNS = IMAGES // QUAD

BANK_USERS = {
    "X": [("b1", B, "maxn", 2), ("a2", A, "k_sum", 1), ("b2", B, "maxn", 4), ("b3", B, "maxn", 6),
          ("d2", DE, "conv_ready", 3), ("e1", DE, "fmaxn", 3)],
    "Y": [("f1", F, "fexp", 2), ("c1", C, "cexp", 2), ("c2", C, "cexp", 4), ("c3", C, "cexp", 6),
          ("c4", C, "cexp", 8), ("b4", B, "mT_ready", 1)],
    "Z": [("p", C, "y_read", 2), ("y1", C, "yn_ready", 1), ("e2", DE, "fmT_ready", 1)],
    "W": [("a1", A, "xnT_ready", 1), ("f2", F, "comb_ready", 1), ("d1", DE, "xn2T_ready", 1),
          ("f3", F, "combT_ready", 1), ("f4", F, "res_ready", 1),
          ("y2", C, "ynT_ready", 1), ("cp", C, "h2_ready", 1)],
}

COUNTS = dict(
    xn_ready=1, xnT_ps=1, xnT_ready=1, q_ps=1, k_ps=1, v_ps=1, q_hi=1, k_sum=1, q_rest=1, k_hi=1, k_rest=1,
    q_mid=1, k_mid=1, q_lo=1, k_lo=1, v_ready=1,
    s_ps=3, maxn=6, m_parts=1, mT_ps=1, mT_ready=1,
    st_ps=4, cexp=8, pv_done=4, y_ps=1, y_read=2, ynat_ps=1, yn_ready=1, ynT_ps=1, ynT_ready=1, proj_ps=1,
    h2_ready=1, xn2_ready=1, xn2T_ps=1, xn2T_ready=1, f_ps=1, fq_ready=1, fk_ready=1,
    conv_ready=3, fv_ready=1, logit_in=1, gmax_in=1, gexp=1, top_in=1, texp=1, w_ready=1, fs_ps=1, fmaxn=3, fm_parts=1, fmT_ps=1,
    fmT_ready=1, fst_ps=1, fexp=2, comb_ps=1, comb_ready=1, combT_ps=1, combT_ready=1, fin_ps=1, res_ready=1,
    var_ready=1, rstd_ready=1, var2_ready=1, rstd2_ready=1)


OWN = dict(norm=4, norm2=4, max=3, fmax=3, comb=2, conv=3, gate=3, gate2=9, yn=1, top=2)


class Step:

    def __init__(self, i, u):
        self.i, self.u = i, u

    def active(self, stage):
        return not isinstance(self.i, int) or 0 <= QUAD * self.i + self.u - stage < IMAGES

    def image(self, stage):
        return self.i * QUAD + (self.u - stage)

    def slot(self, stage, n):
        return (self.u - stage) % n

    def pair(self, stage):
        return self.i * (QUAD // 2) + (self.u - stage) // 2

    def turn(self, stage):
        return self.i + (self.u - stage) // QUAD

    def wait(self, eng, sem, name, stage, count=None, back=0):
        n = self.image(stage + back)
        if isinstance(n, int) and (n < 0 or n >= IMAGES):
            return
        per = COUNTS[name]
        eng.wait_ge(sem[name], n * per + (per if count is None else count))

    def wait_bank(self, eng, sem, bank, segment):
        users = BANK_USERS[bank]
        at = [x[0] for x in users].index(segment)
        for name, stage, counter, count, back in [(*x, 0) for x in users[:at][::-1]] + [(*x, 1) for x in users[::-1]]:
            n = self.image(stage + back)
            if not isinstance(n, int) or 0 <= n < IMAGES:
                eng.wait_ge(sem[counter], n * COUNTS[counter] + count)
                return


def steps(eng):
    for i in range(PRE):
        for u in range(QUAD):
            yield Step(i, u)
    with eng.Fori(PRE, TURNS - 1) as i:
        for u in range(QUAD):
            yield Step(i, u)
    for u in range(QUAD + LAST):
        yield Step(TURNS - 1 + u // QUAD, u % QUAD)


class Order:

    def __init__(self, eng, semaphore, per):
        self.eng, self.semaphore, self.per, self.k = eng, semaphore, per, 0

    def begin(self, n):
        assert self.k in (0, self.per), self.k
        self.n, self.k = n, 0

    def mark(self, ins):
        self.k += 1
        ins.then_inc(self.semaphore, 1)

    def wait(self, but=0):
        self.eng.wait_ge(self.semaphore, self.n * self.per + self.k - but)


def vit_tower(nc, xt, xc, wtok, t97, t128, out):
    ctx = ExitStack()
    with ctx:
        def sb(name, shape, dt=F32):
            return ctx.enter_context(nc.sbuf_tensor(name, shape, dt))

        def psum(name, shape):
            return ctx.enter_context(nc.psum_tensor(name, shape, F32))

        def semaphore(name):
            return ctx.enter_context(nc.semaphore(name))

        h_dram = nc.dram_tensor("h_tokens", (IMAGES, GRID, GRID, D), F32, kind="Internal").ap()

        X = psum("X", [128, 3, 512])
        Y = psum("Y", [128, 2, 512])
        Z = psum("Z", [128, 2, 512])
        W = psum("W", [128, 512])
        Y16 = Y[:, 0, :].bitcast(BF16)
        Z16 = Z[:, 1, :].bitcast(BF16)

        w97 = sb("w97", [97, N97])
        w128 = sb("w128", [128, N128])
        ident16 = sb("ident16", [128, 128], BF16)
        maskn16 = sb("maskn16", [TB, 4 * TB], BF16)
        maskt16 = sb("maskt16", [TB, 3 * TB], BF16)
        sel16 = sb("sel16", [9, E, TB], BF16)
        convs = sb("convs", [ED, 4])
        mhalf = sb("mhalf", [TB, 2])

        xnT = sb("xnT", [DH + 1, 2, T])
        xn2T = sb("xn2T", [DH + 1, 2, T])
        ynT = sb("ynT", [DH + 1, 2, T])
        combT = sb("combT", [DH + 1, 2, T])
        vaug = sb("vaug", [TB, QUAD, 2, HEADS, 2 * HD])
        kstack = sb("kstack", [STACK + PARTS, QUAD, HEADS, T], BF16)
        vf = sb("vf", [TB, 2, 2, E, ED + 1])
        fkp = sb("fkp", [128, 2, E, T])
        mpad = sb("mpad", [TB, 2, 2 * PARTS * HEADS], BF16)
        mparts = mpad[:, :, 0:PARTS * HEADS].rearrange("p b (a h) -> p b a h", a=PARTS)
        init = semaphore("init")
        INITS = 10

        wq, wk, wv, wproj, wp = (w97[:, C97[n]].rearrange("p (h n) -> p h n", h=2)
                                 for n in ("wq", "wk", "wv", "wproj", "wp"))
        fqk = w97[:, C97["fqk"]].rearrange("p (h n) -> p h n", h=2)
        fvg = w97[:, C97["fvg"]].rearrange("p (h n) -> p h n", h=2)
        rel = w97[0:DH, C97["rel"]]
        ident = w128[:, C128["ident"]]
        keep = w128[:, C128["keep"]]
        tokb = w128[:, C128["tokb"]]
        wg2 = w128[0:TB, C128["wg2"]].rearrange("p (e g) -> p e g", e=E)
        bg2 = w128[0:TB, C128["bg2"]]

        def contract(half):
            return DH + 1 if half == 0 else DH

        sem = {name: semaphore(name) for name in COUNTS}
        t97_in = semaphore("t97_in")
        t128_in = semaphore("t128_in")
        weights_in = semaphore("weights_in")
        consts_ready = semaphore("consts_ready")
        variants_made = semaphore("variants_made")
        x_in = [semaphore(f"x_in{u}") for u in range(SUBS)]
        tok_ps = semaphore("tok_ps")
        tok_sum = semaphore("tok_sum")
        h_out = [semaphore(f"h_out{k}") for k in range(4)]
        corner_in = semaphore("corner_in")
        corner_ps = semaphore("corner_ps")
        corner_sum = semaphore("corner_sum")
        corner_out = semaphore("corner_out")
        h_in = [semaphore(f"h_in{k}") for k in range(QUAD)]
        stack_in = [semaphore(f"stack_in{k}") for k in range(QUAD)]
        mrow_in = [semaphore(f"mrow_in{k}") for k in range(QUAD)]
        res_out = [semaphore(f"res_out{k}") for k in range(2)]
        kept = semaphore("kept")
        own_weights = semaphore("own_weights")
        own_sem = {name: semaphore("own_" + name) for name in OWN}
        tok = ExitStack()
        with tok:
            def tb(name, shape, dt=F32):
                return tok.enter_context(nc.sbuf_tensor(name, shape, dt))

            wraw = tb("wraw", [CH, COPIES, CHUNKS, D])
            weff = tb("weff", [CH, len(VARIANTS), D])
            xts = tb("xts", [CH, SUBS, CHUNKS, PER_SUB * TILE])
            xcs = tb("xcs", [CH, 4, CHUNKS, IMAGES])
            hos = tb("hos", [TILE, 4, 2, D])
            hcs = tb("hcs", [IMAGES, 4, D])

            def tok_bank(pair):
                return (Y, Z)[pair % 4 // 2][0:TILE, pair % 2, 0:2 * D]

            with nc.Block() as block:
                @block.sync
                def _(sp):
                    sp.dma_start(wraw[:, :, :, :].rearrange("p a b c -> p (a b c)"), wtok).then_inc(weights_in, 16)
                    sp.dma_start(w128[:, :], t128).then_inc(t128_in, 16)
                    for u in range(SUBS):
                        sp.dma_start(xts[:, u, :, :].rearrange("p a b -> p (a b)"), xt[0, u]).then_inc(x_in[u], 16)
                    sp.dma_start(w97[:, :], t97).then_inc(t97_in, 16)
                    sp.dma_start(xcs[:, :, :, :].rearrange("p a b c -> p (a b c)"), xc).then_inc(corner_in, 16)
                    with sp.Fori(1, GROUPS) as g:
                        for u in range(SUBS):
                            sp.wait_ge(tok_ps, (g - 1) * (2 * SUBS) + 2 * (u + 1))
                            sp.dma_start(xts[:, u, :, :].rearrange("p a b -> p (a b)"),
                                         xt[g, u]).then_inc(x_in[u], 16)

                @block.tensor
                def _(pe):
                    def tile_product(bank, x, n, rc, cc):
                        for c in range(CHUNKS):
                            mm = nc.tensor.matmul(bank, x[:, c, n], weff[:, variant(rc, cc, c), :],
                                                  start=(c == 0), stop=(c == CHUNKS - 1))
                        return mm

                    def group(g):
                        for u in range(SUBS):
                            pe.wait_ge(x_in[u], g * 16 + 16)
                            if isinstance(g, int):
                                pe.wait_ge(variants_made, PLAIN if u < SUBS - 1 else len(VARIANTS))
                            for p in range(2):
                                if not (isinstance(g, int) and 2 * u + p < 4):
                                    pe.wait_ge(tok_sum, g * (2 * SUBS) + (2 * u + p - 3))
                                for j in range(2):
                                    at = 2 * p + j
                                    rc, cc = TILE_CLASS[u * PER_SUB + at]
                                    mm = tile_product(tok_bank(2 * u + p)[:, j * D:(j + 1) * D], xts[:, u],
                                                      slice(at * TILE, (at + 1) * TILE), rc, cc)
                                mm.then_inc(tok_ps, 1)

                    group(0)
                    with pe.Fori(1, GROUPS) as g:
                        group(g)
                    pe.wait_ge(corner_in, 16)
                    for k, (rc, cc) in enumerate(CORNERS):
                        mm = tile_product(X[0:IMAGES, k // 2, (k % 2) * D:(k % 2 + 1) * D], xcs[:, k],
                                          slice(0, IMAGES), rc, cc)
                        mm.then_inc(corner_ps, 1)

                @block.vector
                def _(dve):
                    dve.wait_ge(weights_in, 16)
                    dve.wait_ge(t128_in, 16)
                    for v0 in range(0, len(VARIANTS), PLAIN):
                        some = range(v0, min(v0 + PLAIN, len(VARIANTS)))
                        for k in range(1, COPIES):
                            for n, v in enumerate(some):
                                rh, _, c3, _ = VARIANTS[v]
                                c = rh * 3 + c3
                                if k > 1:
                                    dve.wait_ge(own_weights, 3 * v0 + (k - 2) * len(some) + n + 1)
                                ins = nc.vector.scalar_tensor_tensor(
                                    out=weff[:, v, :], in0=wraw[:, k, c, :], scalar=keep[:, 4 * v + k - 1:4 * v + k],
                                    in1=wraw[:, 0, c, :] if k == 1 else weff[:, v, :], op0=ALU.mult, op1=ALU.add)
                                ins.then_inc(own_weights if k < COPIES - 1 else variants_made, 1)

                    def evacuate(g, pair):
                        k = pair % 4
                        dve.wait_ge(tok_ps, g * (2 * SUBS) + pair + 1)
                        if not (isinstance(g, int) and pair < 4):
                            dve.wait_ge(h_out[k], g * 64 + (32 if pair >= 4 else 0))
                        nc.vector.tensor_tensor(hos[:, k, :, :].rearrange("p a b -> p (a b)"), tok_bank(pair),
                                                tokb[0:TILE, :], ALU.add).then_inc(tok_sum, 1)

                    for pair in range(2 * SUBS):
                        evacuate(0, pair)
                    with dve.Fori(1, GROUPS) as g:
                        for pair in range(2 * SUBS):
                            evacuate(g, pair)
                    for k in range(2):
                        dve.wait_ge(corner_ps, 2 * k + 2)
                        nc.vector.tensor_tensor(hcs[:, 2 * k:2 * k + 2, :].rearrange("p a b -> p (a b)"),
                                                X[0:IMAGES, k, 0:2 * D], tokb[0:IMAGES, :],
                                                ALU.add).then_inc(corner_sum, 1)
                    dve.wait_ge(t97_in, 16)
                    nc.vector.tensor_copy(ident16[:, :], ident).then_inc(consts_ready, 1)
                    nc.vector.tensor_copy(maskn16[:, :], w128[0:TB, C128["maskn"]]).then_inc(consts_ready, 1)
                    nc.vector.tensor_copy(maskt16[:, :], w128[0:TB, C128["maskt"]]).then_inc(consts_ready, 1)
                    nc.vector.tensor_copy(sel16[:, :, :].rearrange("p a b -> p (a b)"),
                                          w128[0:9, C128["sel"]]).then_inc(consts_ready, 1)
                    nc.vector.tensor_scalar(convs[:, :], w128[0:ED, C128["conv"]], ED ** -0.5, None,
                                            ALU.mult).then_inc(consts_ready, 1)
                    nc.vector.memset(mhalf[:, :], -0.5).then_inc(consts_ready, 1)

                @block.gpsimd
                def _(pool):
                    ones = [t[DH:DH + 1, :, :] for t in (xnT, xn2T, ynT, combT)]
                    ones += [kstack[STACK:STACK + PARTS, :, :, :], vaug[:, :, :, :, HD:2 * HD], vf[:, :, :, :, ED:ED + 1]]
                    zeros = [fkp[ED:128, :, 0:E:2, :], fkp[0:ED, :, 1, :], mpad[:, :, :]]
                    for n, (t, value) in enumerate([(t, 1.0) for t in ones] + [(t, 0.0) for t in zeros]):
                        if n:
                            pool.wait_ge(init, n)
                        nc.gpsimd.memset(t, value).then_inc(init, 1)
                    pool.wait_ge(init, INITS)

                @block.scalar
                def _(act):
                    def store(g, pair):
                        k = pair % 4
                        act.wait_ge(tok_sum, g * (2 * SUBS) + pair + 1)
                        images = h_dram[bass.ds(g * GROUP, GROUP)]
                        for j in range(2):
                            at = 2 * pair + j
                            if at < INNER:
                                to = images[:, 1:1 + INNER, at + 1, :]
                            else:
                                to = [images[:, 0, 1:1 + INNER, :], images[:, GRID - 1, 1:1 + INNER, :],
                                      images[:, 1:1 + INNER, 0, :], images[:, 1:1 + INNER, GRID - 1, :]][at - INNER]
                            act.dma_start(to, hos[:, k, j, :]).then_inc(h_out[k], 16)

                    for pair in range(2 * SUBS):
                        store(0, pair)
                    with act.Fori(1, GROUPS) as g:
                        for pair in range(2 * SUBS):
                            store(g, pair)
                    for k, (rc, cc) in enumerate(CORNERS):
                        act.wait_ge(corner_sum, k // 2 + 1)
                        act.dma_start(h_dram[:, CORNER_AT[rc], CORNER_AT[cc], :],
                                      hcs[:, k, :]).then_inc(corner_out, 16)
                    for k in range(4):
                        act.wait_ge(h_out[k], GROUPS * 64)
                    act.wait_ge(corner_out, 64)

        ha = sb("ha", [TB, QUAD, 2, D])
        h2 = sb("h2", [TB, QUAD, 2, D])
        xn = sb("xn", [TB, 2, D])
        xn2 = sb("xn2", [TB, 2, D])
        stat = sb("stat", [TB, 2, 6])
        mv = sb("mv", [TB, 2, 2])
        rstd = sb("rstd", [TB, 2])
        vare = sb("vare", [TB, 2])
        stat2 = sb("stat2", [TB, 2, 6])
        mv2 = sb("mv2", [TB, 2, 2])
        rstd2 = sb("rstd2", [TB, 2])
        vare2 = sb("vare2", [TB, 2])
        qparts = sb("qparts", [DH, 2, PARTS, 2 * T], BF16)
        kparts = sb("kparts", [DH, 2, PARTS, 2 * T], BF16)
        qrest = sb("qrest", [DH, 2 * T])
        ksum = sb("ksum", [DH, 2 * T])
        krest = sb("krest", [DH, 2 * T])
        qstack = sb("qstack", [STACK + PARTS, QUAD, HEADS, T], BF16)
        mx = sb("mx", [TB, 2, HEADS])
        mrest = sb("mrest", [TB, 2, HEADS])
        mT = sb("mT", [PARTS * HEADS, 2, T], BF16)
        probs = sb("probs", [TB, 2, 2, 490])
        yT = sb("yT", [128, 3, T])
        rden = sb("rden", [TB, 2, HEADS])
        yn = sb("yn", [TB, 2, D])
        fq01 = sb("fq01", [128, 2, T])
        fq2 = sb("fq2", [128, 2, T])
        conv_t = sb("conv_t", [ED, T])
        gl = sb("gl", [TB, 2, E, GATE])
        gate = sb("gate", [TB, 12, 2, E])
        gs = sb("gs", [TB, 8, 2])
        wexp = sb("wexp", [TB, 2, 2, E])
        fmx = sb("fmx", [TB, 2, E])
        fmrest = sb("fmrest", [TB, 2, E])
        fmparts = sb("fmparts", [TB, 2, PARTS, E], BF16)
        fmT = sb("fmT", [PARTS * E, 2, T], BF16)
        fprobs = sb("fprobs", [TB, 2, 490])
        fden = sb("fden", [TB, 2, E])
        fscale = sb("fscale", [TB, 2, E])
        comb = sb("comb", [TB, 2, D])
        res = sb("res", [TB, 2, 2, D])

        PLACE = [((0, 0), (0, T)), ((1, 0), (1, T)), ((0, T + TB), (1, T + TB))]
        USED = [2 * T + TB, 2 * T]

        def wait_ready(eng, st, name, stage, count=None, back=0):
            st.wait(eng, sem, name, stage, count, back)

        with nc.Block() as block:
            @block.sync
            def _(sp):
                def load_h(st):
                    wait_ready(sp, st, "h2_ready", NEXT, back=QUAD)
                    sp.dma_start(ha[:, st.slot(NEXT, QUAD)],
                                 h_dram[st.image(NEXT)].rearrange("(b g) c d -> (g c) b d", b=2)
                                 ).then_inc(h_in[st.slot(NEXT, QUAD)], 16)

                load_h(Step(0, -1))
                for st in steps(sp):
                    if st.active(NEXT):
                        load_h(st)
                    if st.active(A):
                        k = st.slot(A, QUAD)
                        wait_ready(sp, st, "st_ps", A, back=QUAD)
                        wait_ready(sp, st, "q_lo", A)
                        for b, part in enumerate((0, 0, 0, 1, 1, 2)):
                            sp.dma_start(qstack[b * HD:(b + 1) * HD, k], qparts[:, st.slot(A, 2), part, :]
                                         ).then_inc(stack_in[k], 16)
                        wait_ready(sp, st, "k_lo", A)
                        for b, part in enumerate((0, 1, 2, 0, 1, 0)):
                            sp.dma_start(kstack[b * HD:(b + 1) * HD, k], kparts[:, st.slot(A, 2), part, :]
                                         ).then_inc(stack_in[k], 16)
                    if st.active(F):
                        wait_ready(sp, st, "res_ready", F)
                        sp.dma_start(out[st.image(F)].rearrange("(b p) d -> p b d", b=2), res[:, st.slot(F, 2)]
                                     ).then_inc(res_out[st.slot(F, 2)], 16)
                    if st.active(B):
                        wait_ready(sp, st, "mT_ready", B)
                        sp.dma_start(qstack[STACK:STACK + PARTS, st.slot(B, QUAD)], mT[:, st.slot(B, 2), :]
                                     ).then_inc(mrow_in[st.slot(B, QUAD)], 16)
                for k in range(2):
                    sp.wait_ge(res_out[k], IMAGES // 2 * 16)

            @block.gpsimd
            def _(pool):
                def deviation(st, stage, var, r, ready, done):
                    wait_ready(pool, st, ready, stage)
                    nc.gpsimd.tensor_tensor(r[:, :], var[:, :], mhalf[:, :], ALU.pow).then_inc(sem[done], 1)

                deviation(Step(0, -1), NEXT, vare, rstd, "var_ready", "rstd_ready")
                for st in steps(pool):
                    if st.active(A):
                        k = st.slot(A, 2)
                        n = st.image(A + 2)
                        if not isinstance(n, int) or n >= 0:
                            pool.wait_ge(stack_in[st.slot(A + 2, QUAD)], st.turn(A + 2) * 192 + 192)
                        wait_ready(pool, st, "q_mid", A)
                        nc.gpsimd.tensor_tensor(qparts[:, k, 2, :], qrest[:, :], qparts[:, k, 1, :], ALU.subtract
                                                ).then_inc(sem["q_lo"], 1)
                        wait_ready(pool, st, "k_mid", A)
                        nc.gpsimd.tensor_tensor(kparts[:, k, 2, :], krest[:, :], kparts[:, k, 1, :], ALU.subtract
                                                ).then_inc(sem["k_lo"], 1)
                    if st.active(NEXT):
                        deviation(st, NEXT, vare, rstd, "var_ready", "rstd_ready")
                    if st.active(C):
                        deviation(st, C, vare2, rstd2, "var2_ready", "rstd2_ready")

            @block.tensor
            def _(pe):
                def turned(to, x):
                    for half in range(2):
                        for b in range(2):
                            mm = nc.tensor.transpose(to[0:DH, half * T + b * TB:half * T + (b + 1) * TB],
                                                     x[:, b, half * DH:(half + 1) * DH], ident[0:TB, 0:TB])
                    return mm

                def natural(to, xT, w, width):
                    for b in range(2):
                        for half in range(2):
                            mm = nc.tensor.matmul(to[0:TB, b * width:(b + 1) * width],
                                                  xT[0:contract(half), half, b * TB:(b + 1) * TB],
                                                  w[0:contract(half), half, :], start=(half == 0), stop=(half == 1))
                    return mm

                def widths(to, xT, w, at, m):
                    for half in range(2):
                        mm = nc.tensor.matmul(to, w[0:contract(half), half, at:at + m], xT[0:contract(half), half, :],
                                              start=(half == 0), stop=(half == 1))
                    return mm

                def mask(to, table, n, start):
                    return nc.tensor.matmul(to, ident16[0:TB, 0:TB], table[:, 0:n], start=start, stop=False,
                                            skip_group_check=True)

                def add(to, keys_or_queries, others):
                    return nc.tensor.matmul(to, keys_or_queries, others, start=False, stop=True,
                                            skip_group_check=True)

                def masks_transposed():
                    for bank in range(2):
                        mask(Y[0:TB, bank, 0:TB], maskt16, TB, True)
                        mask(Y[0:TB, bank, T:T + 2 * TB], maskt16, 2 * TB, False)

                def f1(st):
                    st.wait_bank(pe, sem, "Y", "f1")
                    masks_transposed()
                    k = st.slot(F, 2)
                    for e in range(E):
                        q = fq2 if e == 2 else fq01
                        for b, (bank, col) in enumerate(PLACE[e]):
                            add(Y[0:TB, bank, col:col + T - b * TB], fkp[:, k, e, b * TB:(b + 1) * TB],
                                q[:, k, b * TB:T])
                    wait_ready(pe, st, "fmT_ready", F)
                    for e in range(E):
                        for b, (bank, col) in enumerate(PLACE[e]):
                            mm = add(Y[0:TB, bank, col:col + T - b * TB], sel16[:, e, :], fmT[:, k, b * TB:T])
                    mm.then_inc(sem["fst_ps"], 1)

                def f2(st):
                    st.wait_bank(pe, sem, "W", "f2")
                    wait_ready(pe, st, "fexp", F)
                    k = st.slot(F, 2)
                    for b in range(2):
                        for e in range(E):
                            to = W[0:TB, (b * E + e) * (ED + 1):(b * E + e + 1) * (ED + 1)]
                            for kb in range(b + 1):
                                bank, col = PLACE[e][kb]
                                col += (b - kb) * TB
                                mm = nc.tensor.matmul(to, fprobs[:, bank, col:col + TB], vf[:, k, kb, e, :],
                                                      start=(kb == 0), stop=(kb == b))
                    mm.then_inc(sem["comb_ps"], 1)

                def f3(st):
                    st.wait_bank(pe, sem, "W", "f3")
                    wait_ready(pe, st, "comb_ready", F)
                    turned(W, comb).then_inc(sem["combT_ps"], 1)

                def f4(st):
                    st.wait_bank(pe, sem, "W", "f4")
                    wait_ready(pe, st, "combT_ready", F)
                    natural(W, combT, wp, D).then_inc(sem["fin_ps"], 1)

                def b_group(st, g):
                    st.wait_bank(pe, sem, "X", f"b{g + 1}")
                    k = st.slot(B, QUAD)
                    if g == 0:
                        pe.wait_ge(stack_in[k], st.turn(B) * 192 + 192)
                    for bank in range(2):
                        mask(X[0:TB, bank, 0:2 * T].rearrange("p (h j) -> p h j", h=2)[:, :, TB:T], maskn16,
                             2 * TB, True)
                    mask(X[0:TB, 2, 0:4 * TB], maskn16, 4 * TB, True)
                    for j in range(4):
                        h = 4 * g + j
                        add(X[0:TB, j // 2, (j % 2) * T:(j % 2 + 1) * T], qstack[0:STACK, k, h, TB:T],
                            kstack[0:STACK, k, h, :])
                        mm = add(X[0:TB, 2, j * TB:(j + 1) * TB], qstack[0:STACK, k, h, 0:TB],
                                 kstack[0:STACK, k, h, 0:TB])
                    mm.then_inc(sem["s_ps"], 1)

                def b4(st):
                    st.wait_bank(pe, sem, "Y", "b4")
                    wait_ready(pe, st, "m_parts", B)
                    for b in range(2):
                        mm = nc.tensor.transpose(Y16[0:2 * PARTS * HEADS, b * TB:(b + 1) * TB], mpad[:, b, :],
                                                 ident16[0:TB, 0:TB])
                    mm.then_inc(sem["mT_ps"], 1)

                def c_group(st, g):
                    st.wait_bank(pe, sem, "Y", f"c{g + 1}")
                    k = st.slot(C, QUAD)
                    if g == 0:
                        pe.wait_ge(mrow_in[k], st.turn(C) * 16 + 16)
                    masks_transposed()
                    for j in range(3):
                        h = 3 * g + j
                        for b, (bank, col) in enumerate(PLACE[j]):
                            mm = add(Y[0:TB, bank, col:col + T - b * TB], kstack[:, k, h, b * TB:(b + 1) * TB],
                                     qstack[:, k, h, b * TB:T])
                    mm.then_inc(sem["st_ps"], 1)

                def p_group(st, g):
                    if g == 0:
                        st.wait_bank(pe, sem, "Z", "p")
                    wait_ready(pe, st, "cexp", C, 2 * g + 2)
                    k = st.slot(C, QUAD)
                    for j in range(3):
                        h = 3 * g + j
                        rows = slice(32 * (h % 4), 32 * (h % 4) + 2 * HD)
                        bank, at = h // 8, (h // 4 % 2) * T
                        for b in range(2):
                            pb, col = PLACE[j][b]
                            mm = nc.tensor.matmul(Z[rows, bank, at + b * TB:at + T], vaug[:, k, b, h, :],
                                                  probs[:, g % 2, pb, col:col + T - b * TB], start=(b == 0),
                                                  stop=(b == 1), skip_group_check=True)
                    mm.then_inc(sem["pv_done"], 1)

                def y1(st):
                    wait_ready(pe, st, "y_read", C)
                    for b in range(2):
                        for g in range(3):
                            mm = nc.tensor.transpose(Z[0:TB, b, g * 128:(g + 1) * 128],
                                                     yT[:, g, b * TB:(b + 1) * TB], ident)
                    mm.then_inc(sem["ynat_ps"], 1)

                def y2(st):
                    st.wait_bank(pe, sem, "W", "y2")
                    wait_ready(pe, st, "yn_ready", C)
                    turned(W, yn).then_inc(sem["ynT_ps"], 1)

                def cp(st):
                    st.wait_bank(pe, sem, "W", "cp")
                    wait_ready(pe, st, "ynT_ready", C)
                    natural(W, ynT, wproj, D).then_inc(sem["proj_ps"], 1)

                def a1(st):
                    st.wait_bank(pe, sem, "W", "a1")
                    wait_ready(pe, st, "xn_ready", A)
                    turned(W, xn).then_inc(sem["xnT_ps"], 1)

                def a2(st):
                    st.wait_bank(pe, sem, "X", "a2")
                    wait_ready(pe, st, "xnT_ready", A)
                    natural(X[:, 2, :], xnT, wv, D).then_inc(sem["v_ps"], 1)
                    for i, (w, name) in enumerate(((wq, "q_ps"), (wk, "k_ps"))):
                        for m in range(2):
                            mm = widths(X[0:DH, i, m * T:(m + 1) * T], xnT, w, m * DH, DH)
                        mm.then_inc(sem[name], 1)

                def d1(st):
                    st.wait_bank(pe, sem, "W", "d1")
                    wait_ready(pe, st, "xn2_ready", DE)
                    turned(W, xn2).then_inc(sem["xn2T_ps"], 1)

                def d2(st):
                    st.wait_bank(pe, sem, "X", "d2")
                    wait_ready(pe, st, "xn2T_ready", DE)
                    for m in range(3):
                        widths(X[:, m // 2, (m % 2) * T:(m % 2 + 1) * T], xn2T, fqk, m * 128, 128)
                    natural(X[:, 2, :], xn2T, fvg, D + GATE).then_inc(sem["f_ps"], 1)

                def f_scores(k, e, q):
                    add(X[0:TB, e // 2, (e % 2) * T:(e % 2 + 1) * T], q[:, k, TB:T], fkp[:, k, e, :])
                    return add(X[0:TB, 2, e * TB:(e + 1) * TB], q[:, k, 0:TB], fkp[:, k, e, 0:TB])

                def e1(st):
                    st.wait_bank(pe, sem, "X", "e1")
                    wait_ready(pe, st, "fk_ready", DE)
                    wait_ready(pe, st, "fq_ready", DE)
                    wait_ready(pe, st, "conv_ready", DE)
                    k = st.slot(DE, 2)
                    mask(X[0:TB, 0, 0:2 * T].rearrange("p (h j) -> p h j", h=2)[:, :, TB:T], maskn16, 2 * TB, True)
                    mask(X[0:TB, 1, TB:T], maskn16, TB, True)
                    mask(X[0:TB, 2, 0:3 * TB], maskn16, 3 * TB, True)
                    for e in range(2):
                        f_scores(k, e, fq01)

                def e1_rest(st):
                    f_scores(st.slot(DE, 2), 2, fq2).then_inc(sem["fs_ps"], 1)

                def e2(st):
                    st.wait_bank(pe, sem, "Z", "e2")
                    wait_ready(pe, st, "fm_parts", DE)
                    for b in range(2):
                        mm = nc.tensor.transpose(Z16[0:PARTS * E, b * TB:(b + 1) * TB],
                                                 fmparts[:, b, :, :].rearrange("p a h -> p (a h)"),
                                                 ident16[0:TB, 0:TB])
                    mm.then_inc(sem["fmT_ps"], 1)

                for st in steps(pe):
                    full = {stage: st.active(stage) for stage in (A, B, C, DE, F)}
                    if full[F]:
                        f1(st)
                    if full[A]:
                        a1(st)
                    if full[B]:
                        b_group(st, 0)
                    if full[C]:
                        c_group(st, 0)
                    if full[F]:
                        f2(st)
                    if full[C]:
                        p_group(st, 0)
                    if full[A]:
                        a2(st)
                    if full[C]:
                        c_group(st, 1)
                    if full[DE]:
                        d1(st)
                    if full[B]:
                        b_group(st, 1)
                    if full[C]:
                        p_group(st, 1)
                        c_group(st, 2)
                    if full[B]:
                        b_group(st, 2)
                    if full[C]:
                        p_group(st, 2)
                    if full[F]:
                        f3(st)
                    if full[C]:
                        c_group(st, 3)
                    if full[DE]:
                        d2(st)
                    if full[C]:
                        p_group(st, 3)
                    if full[F]:
                        f4(st)
                    if full[B]:
                        b4(st)
                    if full[C]:
                        y1(st)
                    if full[DE]:
                        e1(st)
                    if full[C]:
                        y2(st)
                    if full[DE]:
                        e1_rest(st)
                    if full[C]:
                        cp(st)
                    if full[DE]:
                        e2(st)

            @block.scalar
            def _(act):
                def copy(to, x, scale=1.0):
                    return nc.scalar.activation(to, x, ACT.Copy, scale=scale)

                def exp_f(st):
                    wait_ready(act, st, "fst_ps", F)
                    wait_ready(act, st, "comb_ps", F, back=1)
                    for bank in range(2):
                        nc.scalar.activation(fprobs[:, bank, 0:USED[bank]], Y[0:TB, bank, 0:USED[bank]], ACT.Exp
                                             ).then_inc(sem["fexp"], 1)

                def exp_c(st, g):
                    wait_ready(act, st, "st_ps", C, g + 1)
                    if g >= 2:
                        wait_ready(act, st, "pv_done", C, g - 1)
                    else:
                        wait_ready(act, st, "pv_done", C, g + 3, back=1)
                    for bank in range(2):
                        nc.scalar.activation(probs[:, g % 2, bank, 0:USED[bank]], Y[0:TB, bank, 0:USED[bank]], ACT.Exp
                                             ).then_inc(sem["cexp"], 1)

                def turned_in(st, stage, ready, done, to):
                    wait_ready(act, st, ready, stage)
                    copy(to[0:DH, :, :].rearrange("p h t -> p (h t)"), W[0:DH, 0:2 * T]).then_inc(sem[done], 1)

                def project_f(st):
                    wait_ready(act, st, "f_ps", DE)
                    k = st.slot(DE, 2)
                    wait_ready(act, st, "fst_ps", DE, back=2)
                    wait_ready(act, st, "comb_ps", DE, back=2)
                    copy(vf[:, k, :, :, 0:ED],
                         X[0:TB, 2, 0:2 * (D + GATE)].rearrange("p (b n) -> p b n", b=2)[:, :, 0:D]
                         .rearrange("p b (e d) -> p b e d", e=E)).then_inc(sem["fv_ready"], 1)

                def project_f_rest(st):
                    k = st.slot(DE, 2)
                    scale = ED ** -0.5
                    copy(fq01[ED:128, k, :], X[ED:128, 0, 0:T], scale)
                    copy(fq2[:, k, :], X[:, 1, 0:T], scale).then_inc(sem["fq_ready"], 1)
                    copy(fkp[ED:128, k, 1, :], X[ED:128, 0, T:2 * T])
                    copy(fkp[0:ED, k, 2, :], X[ED:128, 1, 0:T]).then_inc(sem["fk_ready"], 1)

                def a_parts(st):
                    wait_ready(act, st, "v_ps", A)
                    wait_ready(act, st, "pv_done", A, back=QUAD)
                    copy(vaug[:, st.slot(A, QUAD), :, :, 0:HD],
                         X[0:TB, 2, 0:2 * D].rearrange("p (b h d) -> p b h d", b=2, h=HEADS)
                         ).then_inc(sem["v_ready"], 1)
                    k = st.slot(A, 2)
                    n = st.image(A + 2)
                    if not isinstance(n, int) or n >= 0:
                        act.wait_ge(stack_in[st.slot(A + 2, QUAD)], st.turn(A + 2) * 192 + 192)
                    wait_ready(act, st, "q_ps", A)
                    copy(qparts[:, k, 0, :], X[0:DH, 0, 0:2 * T], HD ** -0.5).then_inc(sem["q_hi"], 1)
                    wait_ready(act, st, "k_sum", A)
                    copy(kparts[:, k, 0, :], ksum[:, :]).then_inc(sem["k_hi"], 1)

                def a_mids(st):
                    k = st.slot(A, 2)
                    wait_ready(act, st, "q_rest", A)
                    copy(qparts[:, k, 1, :], qrest[:, :]).then_inc(sem["q_mid"], 1)
                    wait_ready(act, st, "k_rest", A)
                    copy(kparts[:, k, 1, :], krest[:, :]).then_inc(sem["k_mid"], 1)

                def max_rows(st):
                    wait_ready(act, st, "mT_ps", B)
                    n = st.image(B + 2)
                    if not isinstance(n, int) or n >= 0:
                        act.wait_ge(mrow_in[st.slot(B + 2, QUAD)], st.turn(B + 2) * 16 + 16)
                    copy(mT[:, st.slot(B, 2), :], Y16[0:PARTS * HEADS, 0:T]).then_inc(sem["mT_ready"], 1)

                def sums_out(st):
                    wait_ready(act, st, "pv_done", C)
                    wait_ready(act, st, "ynat_ps", C, back=1)
                    copy(yT[:, 0:2, :].rearrange("p g t -> p (g t)"), Z[:, 0, 0:2 * T]).then_inc(sem["y_read"], 1)
                    copy(yT[:, 2, :], Z[:, 1, 0:T]).then_inc(sem["y_read"], 1)

                def gate_exp(st, to, x, ready, done):
                    wait_ready(act, st, ready, DE)
                    nc.scalar.activation(gate[:, to, :, :], gate[:, x, :, :], ACT.Exp).then_inc(sem[done], 1)

                for st in steps(act):
                    full = {stage: st.active(stage) for stage in (A, B, C, DE, F)}
                    if full[F]:
                        exp_f(st)
                    if full[A]:
                        turned_in(st, A, "xnT_ps", "xnT_ready", xnT)
                    if full[C]:
                        exp_c(st, 0)
                    if full[A]:
                        a_parts(st)
                    if full[C]:
                        exp_c(st, 1)
                    if full[A]:
                        a_mids(st)
                    if full[DE]:
                        turned_in(st, DE, "xn2T_ps", "xn2T_ready", xn2T)
                    if full[C]:
                        exp_c(st, 2)
                    if full[F]:
                        turned_in(st, F, "combT_ps", "combT_ready", combT)
                    if full[C]:
                        exp_c(st, 3)
                    if full[DE]:
                        project_f(st)
                    if full[C]:
                        sums_out(st)
                    if full[DE]:
                        project_f_rest(st)
                    if full[B]:
                        max_rows(st)
                    if full[C]:
                        turned_in(st, C, "ynT_ps", "ynT_ready", ynT)
                    if full[DE]:
                        gate_exp(st, 2, 1, "gmax_in", "gexp")
                        wait_ready(act, st, "fmT_ps", DE)
                        copy(fmT[:, st.slot(DE, 2), :], Z16[0:PARTS * E, 0:T]).then_inc(sem["fmT_ready"], 1)
                        gate_exp(st, 7, 6, "top_in", "texp")

            @block.vector
            def _(dve):
                own = {name: Order(dve, own_sem[name], per) for name, per in OWN.items()}
                def norm_stats(st, stage, x, stats, m, ve, o, done):
                    o.begin(st.image(stage))
                    for b in range(2):
                        o.mark(nc.vector.bn_stats(stats[:, b, :], x[:, b, :]))
                    o.wait()
                    nc.vector.memset(ve[:, :], 0.0)
                    for b in range(2):
                        o.mark(nc.vector.bn_aggr(m[:, b, :], stats[:, b, :]))
                    o.wait()
                    nc.vector.tensor_scalar(ve[:, :], m[:, :, 1], EPS, None, ALU.add).then_inc(sem[done], 1)

                def norm_apply(st, stage, x, m, r, y, rstd_name, turned_name, done):
                    wait_ready(dve, st, rstd_name, stage)
                    wait_ready(dve, st, turned_name, stage, back=1)
                    for b in range(2):
                        ins = nc.vector.tensor_scalar(y[:, b, :], x[:, b, :], m[:, b, 0:1], r[:, b:b + 1],
                                                      ALU.subtract, ALU.mult)
                    ins.then_inc(sem[done], 1)

                def norm_first_stats(st):
                    k = st.slot(NEXT, QUAD)
                    dve.wait_ge(h_in[k], st.turn(NEXT) * 16 + 16)
                    norm_stats(st, NEXT, ha[:, k], stat, mv, vare, own["norm"], "var_ready")

                def norm_first_apply(st):
                    k = st.slot(NEXT, QUAD)
                    norm_apply(st, NEXT, ha[:, k], mv, rstd, xn, "rstd_ready", "xnT_ps", "xn_ready")

                def max_b(st, g):
                    wait_ready(dve, st, "s_ps", B, g + 1)
                    nc.vector.tensor_reduce(mx[:, 1, 4 * g:4 * g + 4].rearrange("p (a b) -> p a b", a=2),
                                            X[0:TB, 0:2, 0:2 * T].rearrange("p a (h j) -> p a h j", h=2),
                                            AX_X, ALU.max).then_inc(sem["maxn"], 1)
                    nc.vector.tensor_reduce(mx[:, 0, 4 * g:4 * g + 4],
                                            X[0:TB, 2, 0:4 * TB].rearrange("p (h j) -> p h j", h=4),
                                            AX_X, ALU.max).then_inc(sem["maxn"], 1)

                def split_max(st, stage, m, rest, parts, maxima, turned_name, done, o):
                    o.begin(st.image(stage))
                    wait_ready(dve, st, maxima, stage)
                    wait_ready(dve, st, turned_name, stage, back=1)
                    o.mark(nc.vector.tensor_scalar(parts[:, :, 0, :], m, -1.0, None, ALU.mult))
                    o.wait()
                    o.mark(nc.vector.scalar_tensor_tensor(out=rest, in0=m, scalar=-1.0, in1=parts[:, :, 0, :],
                                                          op0=ALU.mult, op1=ALU.subtract))
                    o.wait()
                    o.mark(nc.vector.tensor_copy(parts[:, :, 1, :], rest))
                    o.wait()
                    nc.vector.tensor_tensor(parts[:, :, 2, :], rest, parts[:, :, 1, :], ALU.subtract
                                            ).then_inc(sem[done], 1)

                def combine(st):
                    o = own["comb"]
                    o.begin(st.image(F))
                    wait_ready(dve, st, "comb_ps", F)
                    wait_ready(dve, st, "w_ready", F)
                    sums = W[0:TB, 0:2 * E * (ED + 1)].rearrange("p (b e d) -> p b e d", b=2, e=E)
                    o.mark(nc.vector.reciprocal(fden[:, :, :], sums[:, :, :, ED]))
                    o.wait()
                    o.mark(nc.vector.tensor_tensor(fscale[:, :, :], fden[:, :, :], wexp[:, st.slot(F, 2)], ALU.mult))
                    o.wait()
                    wait_ready(dve, st, "combT_ps", F, back=1)
                    nc.vector.tensor_tensor(
                        comb[:, :, :].rearrange("p b (e d) -> p b e d", e=E), sums[:, :, :, 0:ED],
                        fscale[:, :, :].unsqueeze(3).to_broadcast([TB, 2, E, ED]), ALU.mult
                    ).then_inc(sem["comb_ready"], 1)

                def rests(st):
                    wait_ready(dve, st, "q_hi", A)
                    wait_ready(dve, st, "q_lo", A, back=1)
                    wait_ready(dve, st, "v_ready", A)
                    nc.vector.scalar_tensor_tensor(out=qrest[:, :], in0=X[0:DH, 0, 0:2 * T], scalar=HD ** -0.5,
                                                   in1=qparts[:, st.slot(A, 2), 0, :], op0=ALU.mult,
                                                   op1=ALU.subtract).then_inc(sem["q_rest"], 1)
                    wait_ready(dve, st, "k_ps", A)
                    wait_ready(dve, st, "k_hi", A, back=1)
                    nc.vector.tensor_tensor(ksum[:, :], X[0:DH, 1, 0:2 * T], rel, ALU.add).then_inc(sem["k_sum"], 1)
                    wait_ready(dve, st, "k_sum", A)
                    wait_ready(dve, st, "k_hi", A)
                    wait_ready(dve, st, "k_lo", A, back=1)
                    nc.vector.tensor_tensor(krest[:, :], ksum[:, :], kparts[:, st.slot(A, 2), 0, :], ALU.subtract
                                            ).then_inc(sem["k_rest"], 1)

                def convolve(st):
                    o = own["conv"]
                    o.begin(st.image(DE))
                    k = st.slot(DE, 2)
                    wait_ready(dve, st, "f_ps", DE)
                    wait_ready(dve, st, "fst_ps", DE, back=2)
                    q0 = X[0:ED, 0, 0:T]
                    o.mark(nc.vector.tensor_scalar(conv_t[:, :], q0, convs[:, 1:2], convs[:, 3:4], ALU.mult, ALU.add))
                    wait_ready(dve, st, "fv_ready", DE)
                    hidden = X[0:TB, 2, 0:2 * (D + GATE)].rearrange("p (b n) -> p b n", b=2)[:, :, D:D + GATE]
                    for b in range(2):
                        ins = nc.vector.scalar_tensor_tensor(
                            out=gl[:, b, :, :], in0=hidden[:, b, :].unsqueeze(1).to_broadcast([TB, E, GATE]),
                            scalar=0.0, in1=wg2, op0=ALU.max, op1=ALU.mult)
                    o.mark(ins)
                    o.wait(1)
                    o.mark(nc.vector.scalar_tensor_tensor(out=conv_t[:, 1:T], in0=q0[:, 0:T - 1],
                                                          scalar=convs[:, 0:1], in1=conv_t[:, 1:T],
                                                          op0=ALU.mult, op1=ALU.add))
                    nc.vector.tensor_copy(fkp[0:ED, k, 0, :], X[0:ED, 0, T:2 * T]).then_inc(sem["conv_ready"], 1)
                    o.wait()
                    nc.vector.scalar_tensor_tensor(out=fq01[0:ED, k, 0:T - 1], in0=q0[:, 1:T],
                                                   scalar=convs[:, 2:3], in1=conv_t[:, 0:T - 1],
                                                   op0=ALU.mult, op1=ALU.add).then_inc(sem["conv_ready"], 1)
                    nc.vector.tensor_copy(fq01[0:ED, k, T - 1:T], conv_t[:, T - 1:T]).then_inc(sem["conv_ready"], 1)

                def max_e(st):
                    wait_ready(dve, st, "fs_ps", DE)
                    nc.vector.tensor_reduce(fmx[:, 1, 0:2], X[0:TB, 0, 0:2 * T].rearrange("p (h j) -> p h j", h=2),
                                            AX_X, ALU.max).then_inc(sem["fmaxn"], 1)
                    nc.vector.tensor_reduce(fmx[:, 1, 2:3], X[0:TB, 1, 0:T], AX_X, ALU.max
                                            ).then_inc(sem["fmaxn"], 1)
                    nc.vector.tensor_reduce(fmx[:, 0, :], X[0:TB, 2, 0:E * TB].rearrange("p (h j) -> p h j", h=E),
                                            AX_X, ALU.max).then_inc(sem["fmaxn"], 1)

                def wide(x):
                    return x.unsqueeze(2).to_broadcast([TB, 2, E])

                g = [gate[:, i, :, :] for i in range(12)]

                def gate_first(st):
                    o = own["gate"]
                    o.begin(st.image(DE))
                    dve.wait_ge(own_sem["conv"], own["conv"].n * OWN["conv"] + OWN["conv"])
                    o.mark(nc.vector.tensor_reduce(g[0], gl[:, :, :, :], AX_X, ALU.add))
                    o.wait()
                    o.mark(nc.vector.tensor_tensor(g[3], g[0], bg2.rearrange("p (b e) -> p b e", b=2), ALU.add))
                    o.wait()
                    o.mark(nc.vector.tensor_reduce(gs[:, 0, :], g[3], AX_X, ALU.max))
                    o.wait()
                    nc.vector.tensor_tensor(g[1], g[3], wide(gs[:, 0, :]), ALU.subtract).then_inc(sem["gmax_in"], 1)

                def gate_top(st):
                    o = own["gate2"]
                    o.begin(st.image(DE))
                    wait_ready(dve, st, "gexp", DE)
                    o.mark(nc.vector.tensor_reduce(gs[:, 1, :], g[2], AX_X, ALU.add))
                    o.wait()
                    o.mark(nc.vector.reciprocal(gs[:, 2, :], gs[:, 1, :]))
                    o.wait()
                    o.mark(nc.vector.tensor_tensor(g[4], g[2], wide(gs[:, 2, :]), ALU.mult))
                    o.wait()
                    o.mark(nc.vector.tensor_reduce(gs[:, 6, :], g[4], AX_X, ALU.max))
                    o.mark(nc.vector.tensor_tensor(gs[:, 3, :], g[4][:, :, 0], g[4][:, :, 1], ALU.min))
                    o.mark(nc.vector.tensor_tensor(gs[:, 4, :], g[4][:, :, 1], g[4][:, :, 2], ALU.min))
                    o.wait(2)
                    nc.vector.tensor_tensor(g[6], g[4], wide(gs[:, 6, :]), ALU.subtract).then_inc(sem["top_in"], 1)
                    o.wait()
                    o.mark(nc.vector.tensor_tensor(g[5][:, :, 2], g[4][:, :, 2], gs[:, 3, :], ALU.is_gt))
                    o.mark(nc.vector.tensor_tensor(g[5][:, :, 0], g[4][:, :, 0], gs[:, 4, :], ALU.is_ge))
                    o.wait()
                    o.mark(nc.vector.tensor_tensor(gs[:, 5, :], g[5][:, :, 0], g[5][:, :, 2], ALU.add))
                    o.wait()

                def gate_last(st):
                    o = own["top"]
                    o.begin(st.image(DE))
                    nc.vector.tensor_scalar(g[5][:, :, 1], gs[:, 5, :], -1.0, 2.0, ALU.mult, ALU.add
                                            ).then_inc(kept, 1)
                    dve.wait_ge(kept, st.image(DE) * 2 + 1)
                    wait_ready(dve, st, "texp", DE)
                    nc.vector.tensor_tensor(g[8], g[7], g[5], ALU.mult).then_inc(kept, 1)
                    dve.wait_ge(kept, st.image(DE) * 2 + 2)
                    o.mark(nc.vector.tensor_reduce(gs[:, 7, :], g[8], AX_X, ALU.add))
                    o.wait()
                    o.mark(nc.vector.reciprocal(gs[:, 0, :], gs[:, 7, :]))
                    o.wait()
                    nc.vector.tensor_tensor(wexp[:, st.slot(DE, 2)], g[8], wide(gs[:, 0, :]), ALU.mult
                                            ).then_inc(sem["w_ready"], 1)

                def recombine(st):
                    o = own["yn"]
                    o.begin(st.image(C))
                    wait_ready(dve, st, "ynat_ps", C)
                    sums = Z[0:TB, :, 0:2 * D].rearrange("p b (h d) -> p b h d", h=HEADS)
                    o.mark(nc.vector.reciprocal(rden[:, :, :], sums[:, :, :, HD]))
                    o.wait()
                    wait_ready(dve, st, "ynT_ps", C, back=1)
                    nc.vector.tensor_tensor(
                        yn[:, :, :].rearrange("p b (h d) -> p b h d", h=HEADS), sums[:, :, :, 0:HD],
                        rden[:, :, :].unsqueeze(3).to_broadcast([TB, 2, HEADS, HD]), ALU.mult
                    ).then_inc(sem["yn_ready"], 1)

                def both(x):
                    return x.rearrange("p b d -> p (b d)")

                def residual_first(st):
                    k = st.slot(C, QUAD)
                    wait_ready(dve, st, "proj_ps", C)
                    nc.vector.tensor_tensor(both(h2[:, k]), W[0:TB, 0:2 * D], both(ha[:, k]), ALU.add
                                            ).then_inc(sem["h2_ready"], 1)
                    wait_ready(dve, st, "h2_ready", C)
                    norm_stats(st, C, h2[:, k], stat2, mv2, vare2, own["norm2"], "var2_ready")

                def residual_last(st):
                    k = st.slot(F, 2)
                    n = st.image(F + 2)
                    if not isinstance(n, int) or n >= 0:
                        dve.wait_ge(res_out[k], st.pair(F + 2) * 16 + 16)
                    wait_ready(dve, st, "fin_ps", F)
                    nc.vector.tensor_tensor(both(res[:, k]), W[0:TB, 0:2 * D], both(h2[:, st.slot(F, QUAD)]), ALU.add
                                            ).then_inc(sem["res_ready"], 1)

                norm_first_stats(Step(0, -1))
                norm_first_apply(Step(0, -1))
                for st in steps(dve):
                    full = {stage: st.active(stage) for stage in (NEXT, A, B, C, DE, F)}
                    if full[B]:
                        max_b(st, 0)
                    if full[F]:
                        combine(st)
                    if full[A]:
                        rests(st)
                    if full[B]:
                        max_b(st, 1)
                    if full[NEXT]:
                        norm_first_stats(st)
                    if full[B]:
                        max_b(st, 2)
                        split_max(st, B, mx[:, :, :], mrest[:, :, :], mparts, "maxn", "mT_ps", "m_parts", own["max"])
                    if full[NEXT]:
                        norm_first_apply(st)
                    if full[DE]:
                        convolve(st)
                    if full[F]:
                        residual_last(st)
                    if full[C]:
                        recombine(st)
                    if full[DE]:
                        gate_first(st)
                        max_e(st)
                        split_max(st, DE, fmx[:, :, :], fmrest[:, :, :], fmparts, "fmaxn", "fmT_ps", "fm_parts",
                                  own["fmax"])
                    if full[C]:
                        residual_first(st)
                    if full[DE]:
                        gate_top(st)
                    if full[C]:
                        norm_apply(st, C, h2[:, st.slot(C, QUAD)], mv2, rstd2, xn2, "rstd2_ready", "xn2T_ps",
                                   "xn2_ready")
                    if full[DE]:
                        gate_last(st)


_COLUMN_CLASSES = {0: "MF", 1: "MFL", 2: "ML"}


def _keeps():
    import numpy as np
    keep = np.ones((CH, len(VARIANTS), COPIES - 1), np.float32)
    pixel_column = np.arange(CH) % 16
    for v, (rh, rv, c3, cv) in enumerate(VARIANTS):
        rc = ("F" if rh == 0 else "L") if rv else "M"
        cc = _COLUMN_CLASSES[c3][cv]
        right = (c3 * 16 + pixel_column) >= 24
        for k, (oh, ow) in enumerate([(0, 0), (8, 0), (0, 8), (8, 8)]):
            if (oh, rc, rh) in ((0, "L", 1), (8, "F", 0)):
                keep[:, v, k] = 0.0
            if ow == 0 and cc == "L":
                keep[right, v, k] = 0.0
            if ow == 8 and cc == "F":
                keep[~right, v, k] = 0.0
    return keep.reshape(CH, -1)


def kernel(**inputs):
    import numpy as np
    import concourse.bacc as bacc
    from concourse.bass_utils import run_bass_kernel_spmd as run

    a = {k: np.asarray(v) for k, v in inputs.items()}

    x = a["x"].reshape(IMAGES, GRID, 2, 8, GRID, 3, 16).transpose(2, 5, 3, 6, 0, 1, 4)
    x = x.reshape(CHUNKS, CH, IMAGES, GRID, GRID)
    xg = x.reshape(CHUNKS, CH, GROUPS, GROUP, GRID, GRID)
    inner = slice(1, GRID - 1)
    tiles = [xg[:, :, :, :, inner, j] for j in range(1, GRID - 1)]
    tiles += [xg[:, :, :, :, 0, inner], xg[:, :, :, :, GRID - 1, inner],
              xg[:, :, :, :, inner, 0], xg[:, :, :, :, inner, GRID - 1]]
    xt = np.stack(tiles, axis=3).reshape(CHUNKS, CH, GROUPS, SUBS, PER_SUB * TILE)
    xt = np.ascontiguousarray(xt.transpose(2, 3, 1, 0, 4)).reshape(GROUPS, SUBS, CH, CHUNKS * PER_SUB * TILE)
    xc = np.stack([x[:, :, :, CORNER_AT[r], CORNER_AT[c]] for r, c in CORNERS])
    xc = np.ascontiguousarray(xc.transpose(2, 0, 1, 3)).reshape(CH, 4 * CHUNKS * IMAGES)

    w = a["L0_tok_W"].reshape(2, 8, 16, COPIES, 3, D).transpose(3, 0, 1, 2, 4, 5)
    w = w.reshape(COPIES, 2, 8, 3, 16, D).transpose(2, 4, 0, 1, 3, 5)
    wtok = np.ascontiguousarray(w).reshape(CH, COPIES * CHUNKS * D)

    def with_bias(w, b):
        n = w.shape[1]
        t = np.zeros((DH + 1, 2, n), np.float32)
        t[0:DH] = w.reshape(2, DH, n).transpose(1, 0, 2)
        t[DH, 0] = b
        return t.reshape(DH + 1, 2 * n)

    def head_columns(m):
        return m.reshape(m.shape[0], H6, 2, HD).transpose(0, 2, 3, 1).reshape(m.shape[0], D)

    wa, ba = a["L0_attn_w_attn"], a["L0_attn_b_attn"].reshape(1, 3 * D)
    t97 = np.zeros((DH + 1, N97), np.float32)
    for i, name in enumerate(("wq", "wk")):
        part = slice(i * D, (i + 1) * D)
        t97[:, C97[name]] = with_bias(head_columns(wa[:, part]), head_columns(ba[:, part])[0])
    t97[:, C97["wv"]] = with_bias(wa[:, 2 * D:], ba[0, 2 * D:])
    t97[:, C97["wproj"]] = with_bias(a["L0_attn_w_proj"], a["L0_attn_b_proj"])
    t97[:, C97["wp"]] = with_bias(a["L0_ffn_Wp"], a["L0_ffn_bp"])
    wqk, bqk = a["L0_ffn_Wqk"], a["L0_ffn_bqk"].reshape(1, 2 * D)

    def pairs(m):
        return np.concatenate([m[:, 0:2 * ED], m[:, D:D + 2 * ED], m[:, 2 * ED:D], m[:, D + 2 * ED:]], axis=1)

    t97[:, C97["fqk"]] = with_bias(pairs(wqk), pairs(bqk)[0])
    wv = a["L0_ffn_Wv"].transpose(1, 0, 2).reshape(D, D)
    t97[:, C97["fvg"]] = with_bias(np.concatenate([wv, a["L0_ffn_Wg1"]], axis=1),
                                   np.concatenate([a["L0_ffn_bv"].reshape(D), a["L0_ffn_bg1"]]))
    relT = np.zeros((HD, T), np.float32)
    relT[:, 1:] = a["L0_attn_rel_emb"][0:T - 1].T
    t97[0:DH, C97["rel"]] = np.broadcast_to(relT[:, None, None, :], (HD, H6, 2, T)).reshape(DH, 2 * T)

    t128 = np.zeros((128, N128), np.float32)
    t128[:, C128["ident"]] = np.eye(128, dtype=np.float32)
    before = np.arange(TB)[:, None] < np.arange(TB)[None, :]
    t128[0:TB, C128["maskn"]] = np.tile(np.where(before, np.float32(-1e38), np.float32(0)), (1, 4))
    t128[0:TB, C128["maskt"]] = np.tile(np.where(before.T, np.float32(-1e38), np.float32(0)), (1, 3))
    sel = np.zeros((PARTS, E, E, TB), np.float32)
    for e in range(E):
        sel[:, e, e] = 1.0
    t128[0:PARTS * E, C128["sel"]] = sel.reshape(PARTS * E, E * TB)
    t128[:, C128["tokb"]] = np.tile(a["L0_tok_b"], 2)[None]
    t128[0:ED, C128["conv"]] = np.concatenate([a["L0_ffn_conv_w"].reshape(ED, 3),
                                               a["L0_ffn_conv_b"].reshape(ED, 1)], axis=1)
    t128[:, C128["wg2"]] = a["L0_ffn_Wg2"].T.reshape(1, E * GATE)
    t128[:, C128["bg2"]] = np.tile(a["L0_ffn_bg2"], 2)[None]
    t128[:, C128["keep"]] = _keeps()

    nc = bacc.Bacc("TRN2", target_bir_lowering=False, num_devices=1)
    arrays = dict(xt=xt, xc=xc, wtok=wtok, t97=t97, t128=t128)
    aps = [nc.dram_tensor(n, v.shape, F32, kind="ExternalInput").ap() for n, v in arrays.items()]
    out = nc.dram_tensor("out", (IMAGES, T, D), F32, kind="ExternalOutput").ap()
    vit_tower(nc, *aps, out)
    r = run(nc, [arrays], core_ids=[0])
    return r.results[0]["out"]
```
